# Optimizing a Trainium2 kernel written in Bass

```python
import numpy as np
import jax
import jax.numpy as jnp

def _softmax(x, axis=-1):
    return jax.nn.softmax(x, axis=axis)

def _gelu(x):
    return jax.nn.gelu(x, approximate=True)

def _silu(x):
    return jax.nn.silu(x)

def _sigmoid(x):
    return jax.nn.sigmoid(x)

def _layernorm(x, axis=-1, eps=1e-05):
    m = jnp.mean(x, axis=axis, keepdims=True)
    v = jnp.var(x, axis=axis, keepdims=True)
    return (x - m) / jnp.sqrt(v + eps)

def _scatter_add(tgt, idx, src, axis=0):
    return tgt.at[idx].add(src)

def _segment_sum(src, seg, n):
    return jax.ops.segment_sum(src, seg, n)
kernel_name = 'mk_cond_resid_d2_seqx_r8_59cdbe'

def setup_inputs(seed: int=0):
    np.random.seed(seed)
    _w = jnp.asarray

    def _rec_inputs():
        import jax
        import jax.numpy as jnp
        _rk = jax.random.key(seed)
        x = 7.22e-05 + 1 * jax.random.normal(jax.random.fold_in(_rk, 1), (8, 128, 256), jnp.float32)
        _lenS = 128 - jax.random.randint(jax.random.fold_in(_rk, 7), (8,), 0, max(1, 128 // 4) + 1, jnp.int32)
        _lenS2 = 128 - jax.random.randint(jax.random.fold_in(_rk, 8), (8,), 0, max(1, 128 // 4) + 1, jnp.int32)
        cond_2048 = jax.random.bernoulli(jax.random.fold_in(_rk, 11), 0.5063, (8, 256)).astype(jnp.float32)
        return (x, cond_2048)
    x, cond_2048 = _rec_inputs()

    def _L0_cond_setup():
        import jax, jax.numpy as jnp
        import numpy as np
        NH = 8
        NEG = -1e+30
        key = jax.random.key(seed)
        k1, k2, k3, k4 = jax.random.split(key, 4)
        B, D, T = (4, 128, 256)
        x = jax.random.normal(k1, (B, D, T), dtype=jnp.float32)
        mask = jax.random.randint(k2, (B, T), 0, 2).astype(jnp.float32)
        lim = float(np.sqrt(6.0 / (D + D)))
        Wq = jax.random.uniform(k3, (D, D), dtype=jnp.float32, minval=-lim, maxval=lim)
        Wo = jax.random.uniform(k4, (D, D), dtype=jnp.float32, minval=-lim, maxval=lim)
        return {'x': x, 'mask': mask, 'Wq': Wq, 'Wo': Wo}
    _L0_cond_all = _L0_cond_setup()
    _L0_cond_in = {k: v for k, v in _L0_cond_all.items() if k in ('Wq', 'Wo')}
    del _L0_cond_all

    def _L1_cond_setup():
        import jax, jax.numpy as jnp
        import numpy as np
        B, T, D = (16, 128, 256)
        key = jax.random.key(seed)
        k0, k1, k2, k3 = jax.random.split(key, 4)
        scale = 1.0 / np.sqrt(D)
        return {'initial_state': jax.random.normal(k0, (B, D), jnp.float32), 'inputs': jax.random.normal(k1, (B, T, D), jnp.float32), 'W_ih': jax.random.normal(k2, (D, 3 * D), jnp.float32) * scale, 'W_hh': jax.random.normal(k3, (D, 3 * D), jnp.float32) * scale, 'b_ih': jnp.zeros((3 * D,), jnp.float32), 'b_hh': jnp.zeros((3 * D,), jnp.float32)}
    _L1_cond_all = _L1_cond_setup()
    _L1_cond_in = {k: v for k, v in _L1_cond_all.items() if k in ('W_ih', 'W_hh', 'b_ih', 'b_hh')}
    del _L1_cond_all
    return {'x': x, 'cond_2048': cond_2048, 'L0_cond_Wq': _L0_cond_in['Wq'], 'L0_cond_Wo': _L0_cond_in['Wo'], 'L1_cond_W_ih': _L1_cond_in['W_ih'], 'L1_cond_W_hh': _L1_cond_in['W_hh'], 'L1_cond_b_ih': _L1_cond_in['b_ih'], 'L1_cond_b_hh': _L1_cond_in['b_hh']}

def reference(x, cond_2048, L0_cond_Wq, L0_cond_Wo, L1_cond_W_ih, L1_cond_W_hh, L1_cond_b_ih, L1_cond_b_hh):
    import jax
    import jax.numpy as jnp

    def _L0_cond_ref(x, mask, Wq, Wo):
        import jax, jax.numpy as jnp
        import numpy as np
        NH = 8
        NEG = -1e+30
        B, D, T = x.shape
        dk = D // NH
        scale = 1.0 / jnp.sqrt(jnp.asarray(dk, x.dtype))
        xt = jnp.transpose(x, (0, 2, 1))
        q = xt @ Wq.T
        qh = q.reshape(B, T, NH, dk).transpose(0, 2, 1, 3)
        scores = scale * jnp.einsum('bhqd,bhkd->bhqk', qh, qh)
        cmask = mask[:, None, None, :]
        rmask = mask[:, None, :, None]
        logits = (scores * cmask + (1.0 - cmask) * NEG) * rmask
        attn = jax.nn.softmax(logits, axis=-1)
        ctx = jnp.einsum('bhqk,bhkd->bhqd', attn, qh)
        ctx = ctx.transpose(0, 2, 1, 3).reshape(B, T, D)
        out = ctx @ Wo.T
        return jnp.transpose(out, (0, 2, 1))

    def _L1_cond_ref(initial_state, inputs, W_ih, W_hh, b_ih, b_hh):
        import jax, jax.numpy as jnp
        import numpy as np
        B, T, D = (16, 128, 256)
        "ScanOverTime(GRU cell): sequential per-timestep module call with\n            dict-state passing; merge_dict_trees stacks the per-step\n            'state_predicted' tensors along axis=1 -> [B, T, D]."

        def cell(h, x):
            gi = x @ W_ih + b_ih
            gh = h @ W_hh + b_hh
            i_r, i_z, i_n = jnp.split(gi, 3, axis=-1)
            h_r, h_z, h_n = jnp.split(gh, 3, axis=-1)
            r = jax.nn.sigmoid(i_r + h_r)
            z = jax.nn.sigmoid(i_z + h_z)
            n = jnp.tanh(i_n + r * h_n)
            h_new = (1.0 - z) * n + z * h
            return (h_new, h_new)
        xs = jnp.swapaxes(inputs, 0, 1)
        _, hs = jax.lax.scan(cell, initial_state, xs)
        return jnp.swapaxes(hs, 0, 1)
    x = x + _L0_cond_ref(x, cond_2048, L0_cond_Wq, L0_cond_Wo)
    x = x + _L1_cond_ref(cond_2048, x, L1_cond_W_ih, L1_cond_W_hh, L1_cond_b_ih, L1_cond_b_hh)
    return x

_drawn_inputs = setup_inputs


def setup_inputs(seed=0):
    import zlib

    import numpy as np

    out = dict(_drawn_inputs(seed))
    spreads = {'L1_cond_b_ih': (0.0, 0.1), 'L1_cond_b_hh': (0.0, 0.1)}
    factors = {}
    for name, (base, spread) in spreads.items():
        noise = np.random.default_rng([zlib.crc32(name.encode()), seed]).standard_normal(out[name].shape)
        drawn = base * np.exp(spread * noise) if base else spread * noise
        out[name] = jnp.asarray(drawn.astype(out[name].dtype))
    for name, factor in factors.items():
        out[name] = (out[name] * factor).astype(out[name].dtype)
    return out
```

```python
import concourse.bass as bass
from concourse import mybir
from collections import namedtuple
from contextlib import ExitStack


def attention_then_gru(nc, x, x_t, cond, h0_t, wq_t, wo_t, w_ih, w_hh, b_ih, b_hh, out):
    fp32, bf16, fp16, i32 = mybir.dt.float32, mybir.dt.bfloat16, mybir.dt.float16, mybir.dt.int32
    ALU = mybir.AluOpType
    ACT = mybir.ActivationFunctionType
    AX = mybir.AxisListType

    B, D, T = x.shape
    NH = 8
    DK = D // NH
    P = 128
    TC = T // P
    NP = B // 2
    NU = B * NH
    NEG = -1e30
    HALF_SCALE = float(DK) ** -0.25
    KS = 6 * DK
    ROW_MASK, ROW_MAX = KS, KS + 1
    KF = ROW_MAX + 3
    LEAD = 15
    NE = 4

    S = D
    SB = 16
    HB = SB // 2
    BODY = 2 * SB
    G3 = 3 * TC * B
    UP = 64.0

    ctx = ExitStack()
    with ctx:
        def sb(name, shape, dt=fp32):
            return ctx.enter_context(nc.sbuf_tensor(name, shape, dt))

        def sem(name):
            return ctx.enter_context(nc.semaphore(name))

        X = sb("X", [P, B, T])
        XT = sb("XT", [P, TC, (S + SB) * B])
        maskb = sb("maskb", [P, B, T])
        wq = sb("wq", [P, D])
        wqp = sb("wqp", [P, D])
        wo = sb("wo", [P, D])
        mask8 = sb("mask8", [B, T])
        rows8 = sb("rows8", [B, 2, T], bf16)
        ident = sb("ident", [P, P])
        identb = sb("identb", [P, P], bf16)
        ones3 = sb("ones3", [3, 2 * T], bf16)
        onesf = sb("onesf", [1, P])
        qm = sb("qm", [P, 2, 2 * T])
        rest = sb("rest", [P, 2 * T])
        pieces = sb("pieces", [P, 2, 3, 2 * T], bf16)
        KA = [sb(f"KA{i}", [P, NH, 2, T], bf16) for i in range(NP)]
        QB = [sb(f"QB{i}", [P, NH, 2, T], bf16) for i in range(NP)]
        V = sb("V", [P, B, TC, NH, 2 * DK])
        E = sb("E", [P, NE, TC, T])
        nmx = sb("nmx", [P, 2, TC, NH])
        mrest = sb("mrest", [P, TC, NH])
        mpieces = sb("mpieces", [P, 2, TC, 3, NH], bf16)
        mrows = sb("mrows", [3 * NH, 2, T], bf16)
        C = sb("C", [P, 2, T])
        rden = sb("rden", [P, 2, TC, 4])
        Cq = sb("Cq", [P, TC, D])
        CqT = sb("CqT", [P, T])
        Wih = sb("Wih", [P, TC, 3 * T])
        Whh = sb("Whh", [P, TC, 3 * T])
        Whi = sb("Whi", [P, TC, 3 * T], fp16)
        Wlo = sb("Wlo", [P, TC, 3 * T], fp16)
        brow = sb("brow", [1, 4 * T])
        brow2 = sb("brow2", [1, 2 * T])
        bpieces = sb("bpieces", [1, 3, 4 * T], bf16)
        bias3 = sb("bias3", [3, 4 * T], bf16)
        wmax = sb("wmax", [P, 1])
        sc1 = sb("sc1", [1, 8])
        scb = sb("scb", [P, 3])
        h0 = sb("h0", [P, TC * B])
        gate_r = sb("gate_r", [P, G3])
        gate_z = sb("gate_z", [P, G3])
        hs = sb("hs", [P, BODY, G3])
        h16 = [sb(f"h16_{i}", [P, G3], fp16) for i in range(2)]
        ysum = sb("ysum", [P, TC, SB * B])
        yout = sb("yout", [P, 2, T])

        bank = [ctx.enter_context(nc.psum_tensor(f"bank{i}", [P, 512], fp32)) for i in range(8)]
        S1, S2 = bank[0:2], bank[2:4]
        CX, CTB, OW, MT = bank[4], bank[5], bank[6], bank[7]
        R, Z, N = bank[0:2], bank[2:4], bank[4:6]
        PRE, YT = bank[6], bank[7]

        q_dram = nc.dram_tensor("q_pieces", [NP, 3, DK, NH * 2 * T], bf16, kind="Internal").ap()
        rows_dram = nc.dram_tensor("mask_rows", [2, B, T], bf16, kind="Internal").ap()

        names = """ld_x ld_xt ld_mask ld_m8 ld_wq ld_wo ld_whh ld_wih ld_bias ld_h0 const_ready rows_ready
            rows_stored ones_in bias_rows wqp_ready q_done v_done qm_done v_copied p1_done r1_done p2_done p3_done v_ones
            s1_done max_done mp_step mp_done mt_done mt_copied s2_done exp_done av_done c_copied ct_done
            rden_done cq_done cqt_done cqt_copied wo_done xt_done
            wmax_done wmax_row sc_step sc_ready sc_bcast scb_ready w_step w_ready b_step b_ready init_step
            zero_ready r_done z_done scan1_in pre_ready scan2_in high_ready h_ready low_ready
            sum_done y_turned y_copied""".split()
        s = namedtuple("Semaphores", names)(*[sem(n) for n in names])
        q_stored = [sem(f"q_stored{i}") for i in range(NP)]
        stack_in = [sem(f"stack_in{i}") for i in range(NP)]
        mask_in = [sem(f"mask_in{i}") for i in range(NP)]
        mrow_in = [sem(f"mrow_in{i}") for i in range(B)]

        y_free = [sem(f"y_free{i}") for i in range(2)]
        y_stored = [sem(f"y_stored{i}") for i in range(2)]

        block = ctx.enter_context(nc.Block())

        def cols(start, n):
            return slice(start, start + n) if isinstance(start, int) else bass.ds(start, n)

        def gate_cols(t):
            return slice(2 * B * t, 2 * B * (t + 1))

        @block.sync
        def _(sp):
            sp.dma_start(wq[:, :], wq_t).then_inc(s.ld_wq, 16)
            sp.dma_start(X[:, :, :], x.rearrange("b d t -> d b t")).then_inc(s.ld_x, 16)
            sp.dma_start(mask8[:, :], cond).then_inc(s.ld_m8, 16)
            sp.dma_start(Whh[:, :, :], w_hh.rearrange("(c p) n -> p c n", p=P)).then_inc(s.ld_whh, 16)
            sp.wait_ge(s.const_ready, 6)
            for i in range(NP):
                sp.dma_start(KA[i][ROW_MAX:ROW_MAX + 3, :, :, :].rearrange("p h b t -> p h (b t)"),
                             ones3[:, :].unsqueeze(1).to_broadcast([3, NH, 2 * T])).then_inc(s.ones_in, 16)
            sp.wait_ge(s.rows_ready, 2)
            sp.dma_start(rows_dram.rearrange("r b t -> b r t"), rows8[:, :, :]).then_inc(s.rows_stored, 16)
            sp.wait_ge(s.rows_stored, 16)
            for i in range(NP):
                for r, stack in ((0, KA[i]), (1, QB[i])):
                    src = rows_dram[r:r + 1, 2 * i:2 * i + 2, :].rearrange("r b t -> r (b t)")
                    sp.dma_start(stack[ROW_MASK:ROW_MASK + 1, :, :, :].rearrange("p h b t -> p h (b t)"),
                                 src.unsqueeze(1).to_broadcast([1, NH, 2 * T])).then_inc(mask_in[i], 16)
            for i in range(NP):
                sp.wait_ge(q_stored[i], 16)
                flat = q_dram[i].rearrange("k d n -> (k d) n")
                first = 0
                for n in (3, 2, 1):
                    lo, hi = first * DK, (first + n) * DK
                    sp.dma_start(KA[i][lo:hi, :, :, :].rearrange("p h b t -> p (h b t)"),
                                 flat[0:n * DK, :]).then_inc(stack_in[i], 16)
                    piece = q_dram[i][3 - n:4 - n, :, :]
                    sp.dma_start(QB[i][lo:hi, :, :, :].rearrange("p h b t -> p (h b t)"),
                                 piece.to_broadcast([n, DK, NH * 2 * T])).then_inc(stack_in[i], 16)
                    first += n
            for b in range(B):
                sp.wait_ge(s.mt_copied, b + 1)
                for k in range(3):
                    sp.dma_start(QB[b // 2][ROW_MAX + k:ROW_MAX + k + 1, :, b % 2, :],
                                 mrows[k * NH:(k + 1) * NH, b % 2:b % 2 + 1, :]).then_inc(mrow_in[b], 16)
            for p in range(2):
                sp.sem_inc(y_free[p], 1)
            with sp.Fori(0, S // BODY) as turn:
                for p in range(2):
                    sp.wait_ge(s.y_copied, turn * 2 + p + 1)
                    sp.dma_start(out[:, bass.ds(turn * BODY + p * SB, SB), :].rearrange("b t f -> t b f"),
                                 yout[:, p, :]).then_inc(y_stored[p], 16)
                    sp.wait_ge(y_stored[p], turn * 16 + 16)
                    sp.sem_inc(y_free[p], 1)

        @block.gpsimd
        def _(pool):
            pool.memset(ident[:, :], 0.0).then_inc(s.const_ready, 1)
            pool.memset(identb[:, :], 0.0).then_inc(s.const_ready, 1)
            pool.memset(ones3[:, :], 1.0).then_inc(s.const_ready, 1)
            pool.memset(onesf[:, :], 1.0).then_inc(s.const_ready, 1)
            pool.wait_ge(s.const_ready, 4)
            for m in (ident, identb):
                pool.affine_select(out=m[:, :], in_=m[:, :], compare_op=ALU.not_equal, fill=1.0, base=0,
                                   pattern=[[-1, P]], channel_multiplier=1).then_inc(s.const_ready, 1)
            pool.wait_ge(s.ld_m8, 16)
            pool.tensor_scalar(rows8[:, 0, :], mask8[:, :], -1.0, 1.0, ALU.mult, ALU.add).then_inc(s.rows_ready, 1)
            pool.tensor_scalar(rows8[:, 1, :], mask8[:, :], NEG, None, ALU.mult).then_inc(s.rows_ready, 1)
            pool.memset(V[:, :, :, :, DK:2 * DK].rearrange("p b c h k -> p (b c h) k"), 1.0).then_inc(s.v_ones, 1)
            for i in range(NP):
                j = i % 2
                pool.wait_ge(s.p1_done, i + 1)
                pool.tensor_tensor(rest[:, :], qm[:, j, :], pieces[:, j, 0, :], ALU.subtract).then_inc(s.r1_done, 1)
                pool.wait_ge(s.r1_done, i + 1)
                pool.tensor_copy(pieces[:, j, 1, :], rest[:, :]).then_inc(s.p2_done, 1)
                pool.wait_ge(s.p2_done, i + 1)
                pool.tensor_tensor(pieces[:, j, 2, :], rest[:, :], pieces[:, j, 1, :],
                                   ALU.subtract).then_inc(s.p3_done, 1)
                pool.wait_ge(s.p3_done, i + 1)
                pool.dma_start(q_dram[i].rearrange("k d (h n) -> (d h) k n", h=NH),
                               pieces[:, j, :, :]).then_inc(q_stored[i], 16)

            def max_pieces(b):
                j = b % 2
                pool.wait_ge(s.max_done, NH * (b + 1))
                if b >= 2:
                    pool.wait_ge(s.mt_done, b - 1)
                n = 4 * b
                pool.tensor_copy(mpieces[:, j, :, 0, :], nmx[:, j, :, :]).then_inc(s.mp_step, 1)
                pool.wait_ge(s.mp_step, n + 1)
                pool.tensor_tensor(mrest[:, :, :], nmx[:, j, :, :], mpieces[:, j, :, 0, :],
                                   ALU.subtract).then_inc(s.mp_step, 1)
                pool.wait_ge(s.mp_step, n + 2)
                pool.tensor_copy(mpieces[:, j, :, 1, :], mrest[:, :, :]).then_inc(s.mp_step, 1)
                pool.wait_ge(s.mp_step, n + 3)
                pool.tensor_tensor(mpieces[:, j, :, 2, :], mrest[:, :, :], mpieces[:, j, :, 1, :],
                                   ALU.subtract).then_inc(s.mp_step, 1)

            def whh_pieces():
                pool.wait_ge(s.scb_ready, 1)
                pool.wait_ge(s.ld_whh, 16)
                pool.tensor_scalar(Whh[:, :, :], Whh[:, :, :], scb[:, 2:3], None, ALU.mult).then_inc(s.w_step, 1)
                pool.wait_ge(s.w_step, 1)
                pool.tensor_copy(Whi[:, :, :], Whh[:, :, :]).then_inc(s.w_step, 1)
                pool.wait_ge(s.w_step, 2)
                pool.tensor_tensor(Wlo[:, :, :], Whh[:, :, :], Whi[:, :, :], ALU.subtract).then_inc(s.w_ready, 1)

            def wih_and_biases():
                pool.wait_ge(s.ld_wih, 16)
                pool.tensor_scalar(Wih[:, :, :], Wih[:, :, :], UP, None, ALU.mult).then_inc(s.w_ready, 1)
                pool.wait_ge(s.ld_bias, 48)
                pool.tensor_tensor(brow[:, 0:2 * T], brow[:, 0:2 * T], brow2[:, :], ALU.add).then_inc(s.b_step, 1)
                pool.wait_ge(s.b_step, 1)
                pool.tensor_scalar(brow[:, :], brow[:, :], UP, None, ALU.mult).then_inc(s.b_step, 1)
                pool.wait_ge(s.b_step, 2)
                pool.tensor_copy(bpieces[:, 0, :], brow[:, :]).then_inc(s.b_step, 1)
                pool.wait_ge(s.b_step, 3)
                pool.tensor_tensor(brow[:, :], brow[:, :], bpieces[:, 0, :], ALU.subtract).then_inc(s.b_step, 1)
                pool.wait_ge(s.b_step, 4)
                pool.tensor_copy(bpieces[:, 1, :], brow[:, :]).then_inc(s.b_step, 1)
                pool.wait_ge(s.b_step, 5)
                pool.tensor_tensor(bpieces[:, 2, :], brow[:, :], bpieces[:, 1, :], ALU.subtract).then_inc(s.b_step, 1)
                pool.wait_ge(s.b_step, 6)
                pool.dma_start(bias3[:, :], bpieces[:, :, :]).then_inc(s.bias_rows, 16)

            def gru_start():
                pool.memset(XT[:, :, S * B:(S + SB) * B], 0.0).then_inc(s.zero_ready, 1)
                pool.memset(gate_r[:, 0::3], 0.0).then_inc(s.zero_ready, 1)
                pool.memset(gate_r[:, 1::3], 1.0).then_inc(s.zero_ready, 1)
                pool.memset(gate_z[:, 0::3], 0.0).then_inc(s.zero_ready, 1)
                pool.memset(gate_z[:, 1::3], 1.0).then_inc(s.zero_ready, 1)
                pool.memset(hs[:, BODY - 1, 0::3], 0.0).then_inc(s.zero_ready, 1)
                pool.wait_ge(s.zero_ready, 6)
                pool.wait_ge(s.scb_ready, 1)
                pool.tensor_scalar(gate_z[:, 1::3], gate_z[:, 1::3], scb[:, 0:1], None,
                                   ALU.mult).then_inc(s.zero_ready, 1)
                pool.wait_ge(s.ld_h0, 16)
                pool.tensor_scalar(hs[:, BODY - 1, 2::3], h0[:, :], scb[:, 0:1], None,
                                   ALU.mult).then_inc(s.init_step, 1)
                pool.wait_ge(s.init_step, 1)
                pool.tensor_scalar(hs[:, BODY - 1, 1::3], hs[:, BODY - 1, 2::3], -1.0, None,
                                   ALU.mult).then_inc(s.scan2_in, 1)
                pool.tensor_copy(h16[0][:, 2::3], hs[:, BODY - 1, 2::3]).then_inc(s.high_ready, 1)
                pool.wait_ge(s.high_ready, 1)
                pool.tensor_tensor(h16[0][:, 1::3], hs[:, BODY - 1, 2::3], h16[0][:, 2::3],
                                   ALU.subtract).then_inc(s.low_ready, 1)

            max_pieces(0)
            whh_pieces()
            max_pieces(1)
            wih_and_biases()
            max_pieces(2)
            gru_start()
            for b in range(3, B):
                max_pieces(b)

        @block.scalar
        def _(act):
            act.dma_start(maskb[:, :, :].rearrange("p b t -> p (b t)"),
                          cond.rearrange("(o b) t -> o (b t)", o=1).to_broadcast([P, B * T])).then_inc(s.ld_mask, 16)
            act.dma_start(XT[:, :, 0:S * B], x_t).then_inc(s.ld_xt, 16)
            act.dma_start(wo[:, :], wo_t).then_inc(s.ld_wo, 16)
            act.dma_start(Wih[:, :, :], w_ih.rearrange("(c p) n -> p c n", p=P)).then_inc(s.ld_wih, 16)
            act.dma_start(brow[:, 0:3 * T], b_ih).then_inc(s.ld_bias, 16)
            act.dma_start(brow[:, 3 * T:4 * T], b_hh[:, 2 * T:3 * T]).then_inc(s.ld_bias, 16)
            act.dma_start(brow2[:, :], b_hh[:, 0:2 * T]).then_inc(s.ld_bias, 16)
            act.dma_start(h0[:, :], h0_t).then_inc(s.ld_h0, 16)
            for i in range(NP):
                j = i % 2
                act.wait_ge(s.qm_done, i + 1)
                if i >= 2:
                    act.wait_ge(q_stored[i - 2], 16)
                nc.scalar.activation(pieces[:, j, 0, :], qm[:, j, :], ACT.Copy).then_inc(s.p1_done, 1)
                act.wait_ge(s.v_done, i + 1)
                nc.scalar.activation(V[:, 2 * i:2 * i + 2, :, :, 0:DK].rearrange("p b c h k -> p (b c h) k"),
                                     S2[j][:, :].rearrange("p (n k) -> p n k", k=DK), ACT.Copy)\
                    .then_inc(s.v_copied, 1)

            def copy_max(b):
                act.wait_ge(s.mt_done, b + 1)
                if b >= 2:
                    act.wait_ge(mrow_in[b - 2], 48)
                nc.scalar.activation(mrows[:, b % 2, :], MT[0:3 * NH, 0:T], ACT.Copy).then_inc(s.mt_copied, 1)

            def copy_context(b):
                act.wait_ge(s.av_done, NH * (b + 1))
                nc.scalar.activation(C[:, :, :].rearrange("p g t -> p (g t)"), CX[:, :], ACT.Copy)\
                    .then_inc(s.c_copied, 1)

            def copy_turned(b):
                act.wait_ge(s.cqt_done, b + 1)
                nc.scalar.activation(CqT[:, :], OW[:, 0:T], ACT.Copy).then_inc(s.cqt_copied, 1)

            copy_max(0)
            for u in range(NU):
                b, h = u // NH, u % NH
                act.wait_ge(s.s2_done, u + 1)
                if u >= NE:
                    act.wait_ge(s.av_done, u - NE + 1)
                nc.scalar.activation(E[:, u % NE, :, :].rearrange("p c t -> p (c t)"), S2[u % 2][:, :], ACT.Exp)\
                    .then_inc(s.exp_done, 1)
                if h == 2 and b >= 1:
                    copy_context(b - 1)
                if h == 4 and b + 1 < B:
                    copy_max(b + 1)
                if h == 5 and b >= 1:
                    copy_turned(b - 1)
            copy_context(B - 1)
            copy_turned(B - 1)

            def copy_out(turn, p):
                act.wait_ge(y_free[p], turn + 1)
                act.wait_ge(s.y_turned, turn * 2 + p + 1)
                nc.scalar.activation(yout[:, p, :], YT[:, 0:TC * P], ACT.Copy).then_inc(s.y_copied, 1)

            def gates(turn, first=False):
                for t in range(BODY):
                    p, st = t // SB, t % SB
                    act.wait_ge(s.r_done, turn * BODY + t + 1)
                    nc.scalar.activation(gate_r[:, 2::3], R[p][:, gate_cols(st)], ACT.Sigmoid, scale=1.0 / UP)\
                        .then_inc(s.scan1_in, 1)
                    act.wait_ge(s.z_done, turn * BODY + t + 1)
                    nc.scalar.activation(gate_z[:, 2::3], Z[p][:, gate_cols(st)], ACT.Sigmoid, scale=-1.0 / UP)\
                        .then_inc(s.scan2_in, 1)
                    act.wait_ge(s.pre_ready, turn * BODY + t + 1)
                    nc.scalar.activation(hs[:, (t - 1) % BODY, 0::3], PRE[:, 2:G3:3], ACT.Tanh, scale=1.0 / UP)\
                        .then_inc(s.scan2_in, 1)
                    if t == 3 and not first:
                        copy_out(turn - 1, 1)
                    if t == SB + 3:
                        copy_out(turn, 0)

            gates(0, first=True)
            with act.Fori(1, S // BODY) as turn:
                gates(turn)
            copy_out(S // BODY - 1, 1)

        @block.vector
        def _(dve):
            dve.wait_ge(s.ld_wq, 16)
            nc.vector.tensor_copy(wqp[:, :].rearrange("d (k h) -> d k h", h=NH),
                                  wq[:, :].rearrange("d (h k) -> d k h", k=DK)).then_inc(s.wqp_ready, 1)
            dve.wait_ge(s.ld_mask, 16)
            for i in range(NP):
                dve.wait_ge(s.q_done, i + 1)
                if i >= 2:
                    dve.wait_ge(s.p3_done, i - 1)
                nc.vector.scalar_tensor_tensor(
                    qm[:, i % 2, :], S1[i % 2][:, :], HALF_SCALE,
                    maskb[:, 2 * i:2 * i + 2, :].rearrange("p b t -> p (b t)"), ALU.mult, ALU.mult)\
                    .then_inc(s.qm_done, 1)
            dve.wait_ge(s.ld_whh, 16)
            nc.vector.reduce_max(wmax[:, :], Whh[:, :, :].rearrange("p c n -> p (c n)"), AX.X,
                                 apply_absolute_value=True).then_inc(s.wmax_done, 1)
            dve.wait_ge(s.wmax_row, 1)
            nc.vector.reduce_max(sc1[:, 0:1], MT[0:1, 0:P], AX.X).then_inc(s.sc_step, 1)
            dve.wait_ge(s.sc_step, 1)
            nc.vector.tensor_single_scalar(sc1[:, 1:2].bitcast(i32), sc1[:, 0:1].bitcast(i32), 0x7F800000,
                                           ALU.bitwise_and).then_inc(s.sc_step, 1)
            dve.wait_ge(s.sc_step, 2)
            nc.vector.tensor_scalar(sc1[:, 2:3], sc1[:, 1:2], 2.0 ** -8, 1.0, ALU.mult, ALU.max)\
                .then_inc(s.sc_step, 1)
            dve.wait_ge(s.sc_step, 3)
            nc.vector.tensor_scalar(sc1[:, 4:5], sc1[:, 2:3], 2.0 ** 15, None, ALU.min).then_inc(s.sc_step, 1)
            dve.wait_ge(s.sc_step, 4)
            nc.vector.reciprocal(sc1[:, 5:6], sc1[:, 4:5]).then_inc(s.sc_step, 1)
            dve.wait_ge(s.sc_step, 5)
            nc.vector.tensor_scalar(sc1[:, 6:7], sc1[:, 5:6], UP, None, ALU.mult).then_inc(s.sc_ready, 1)
            dve.wait_ge(s.sc_bcast, 1)
            nc.vector.tensor_copy(scb[:, :], MT[:, 128:131]).then_inc(s.scb_ready, 1)

            def row_max(u):
                b, h = u // NH, u % NH
                dve.wait_ge(s.s1_done, u + 1)
                if b >= 2 and h == 0:
                    dve.wait_ge(s.mp_step, 4 * (b - 1))
                nc.vector.reduce_max(nmx[:, b % 2, :, h], S1[u % 2][:, :].rearrange("p (c t) -> p c t", c=TC),
                                     AX.X, negate=True).then_inc(s.max_done, 1)

            def normalise(b):
                turned = CTB[:, :].rearrange("p (g c j k) -> p g c j k", g=2, c=TC, j=4)
                dve.wait_ge(s.ct_done, b + 1)
                nc.vector.reciprocal(rden[:, :, :, :], turned[:, :, :, :, DK]).then_inc(s.rden_done, 1)
                dve.wait_ge(s.rden_done, b + 1)
                for g in range(2):
                    for c in range(TC):
                        nc.vector.tensor_tensor(
                            Cq[:, c, g * 64:(g + 1) * 64].rearrange("p (j k) -> p j k", k=DK),
                            turned[:, g, c, :, 0:DK],
                            rden[:, g, c, :].unsqueeze(2).to_broadcast([P, 4, DK]), ALU.mult).then_inc(s.cq_done, 1)

            def add_residual(b):
                dve.wait_ge(s.wo_done, b + 1)
                xb = XT[:, :, b:S * B:B]
                nc.vector.tensor_tensor(xb, OW[:, T:2 * T].rearrange("p (c d) -> p c d", c=TC), xb, ALU.add)\
                    .then_inc(s.xt_done, 1)

            for u in range(LEAD):
                row_max(u)
            dve.wait_ge(s.ld_xt, 16)
            for u in range(NU):
                b, h = u // NH, u % NH
                if u + LEAD < NU:
                    row_max(u + LEAD)
                if h == 4 and b >= 1:
                    normalise(b - 1)
                if h == 7 and b >= 1:
                    add_residual(b - 1)
            normalise(B - 1)
            add_residual(B - 1)

            dve.wait_ge(s.zero_ready, 7)

            def sum_block(turn, p, c):
                if c == 0:
                    dve.wait_ge(s.h_ready, turn * BODY + SB * (p + 1))
                src = hs[:, SB * p:SB * (p + 1), 24 * c + 2:24 * c + 24:3]
                xx = XT[:, c, cols(turn * (BODY * B) + p * SB * B, SB * B)]
                nc.vector.scalar_tensor_tensor(ysum[:, c, :].rearrange("p (s b) -> p s b", b=B), src, scb[:, 1:2],
                                               xx.rearrange("p (s b) -> p s b", b=B), ALU.mult, ALU.add)\
                    .then_inc(s.sum_done, 1)

            def scans(turn, first=False):
                for t in range(BODY):
                    hh = (t // HB) % 2
                    dve.wait_ge(s.scan1_in, turn * (2 * BODY) + 2 * (t + 1))
                    nc.vector.tensor_tensor_scan(PRE[:, 0:G3], gate_r[:, :],
                                                 N[hh][:, G3 * (t % HB):G3 * (t % HB + 1)], 0.0,
                                                 ALU.mult, ALU.add).then_inc(s.pre_ready, 1)
                    dve.wait_ge(s.scan2_in, turn * (3 * BODY) + 3 * (t + 1))
                    before = hs[:, (t - 1) % BODY, :]
                    nc.vector.tensor_tensor_scan(h16[(t + 1) % 2][:, :], gate_z[:, :], before, 0.0,
                                                 ALU.mult, ALU.add).then_inc(s.high_ready, 1)
                    nc.vector.tensor_tensor_scan(hs[:, t, :], gate_z[:, :], before, 0.0,
                                                 ALU.mult, ALU.add).then_inc(s.h_ready, 1)
                    dve.wait_ge(s.h_ready, turn * BODY + t + 1)
                    nc.vector.tensor_tensor(h16[(t + 1) % 2][:, 1::3], hs[:, t, 2::3], h16[(t + 1) % 2][:, 2::3],
                                            ALU.subtract).then_inc(s.low_ready, 1)
                    nc.vector.tensor_scalar(hs[:, t, 1::3], hs[:, t, 2::3], -1.0, None, ALU.mult)\
                        .then_inc(s.scan2_in, 1)
                    if t < TC and not first:
                        sum_block(turn - 1, 1, t)
                    if SB <= t < SB + TC:
                        sum_block(turn, 0, t - SB)

            scans(0, first=True)
            with dve.Fori(1, S // BODY) as turn:
                scans(turn)
            for c in range(TC):
                sum_block(S // BODY - 1, 1, c)

        @block.tensor
        def _(pe):
            mm = nc.tensor.matmul
            pe.wait_ge(s.ld_wq, 16)
            pe.wait_ge(s.wqp_ready, 1)
            pe.wait_ge(s.ld_x, 16)
            for i in range(NP):
                j = i % 2
                if i >= 2:
                    pe.wait_ge(s.qm_done, i - 1)
                mm(S1[j][:, :], wqp[:, :],
                   X[:, 2 * i:2 * i + 2, :].rearrange("d b t -> d (b t)"), start=True, stop=True)\
                    .then_inc(s.q_done, 1)
                if i >= 2:
                    pe.wait_ge(s.v_copied, i - 1)
                for n in range(2 * TC):
                    b, c = 2 * i + n // TC, n % TC
                    last = mm(S2[j][:, n * P:(n + 1) * P], X[:, b, c * P:(c + 1) * P], wq[:, :],
                              start=True, stop=True)
                last.then_inc(s.v_done, 1)
            pe.wait_ge(s.const_ready, 6)
            pe.wait_ge(s.wmax_done, 1)
            mm(MT[0:1, 0:P], wmax[:, :], ident[:, :], start=True, stop=True).then_inc(s.wmax_row, 1)
            pe.wait_ge(s.sc_ready, 1)
            mm(MT[:, 128:131], onesf[:, :], sc1[:, 4:7], start=True, stop=True).then_inc(s.sc_bcast, 1)

            def stack(tile, rows, h, b, c=None):
                cols = slice(0, T) if c is None else slice(c * P, (c + 1) * P)
                return tile[b // 2][0:rows, h, b % 2, cols]

            def scores_for_max(u):
                b, h = u // NH, u % NH
                if u < 2:
                    pe.wait_ge(s.qm_done, NP)
                else:
                    pe.wait_ge(s.max_done, u - 1)
                if u % (2 * NH) == 0:
                    pe.wait_ge(stack_in[b // 2], 96)
                for c in range(TC):
                    last = mm(S1[u % 2][:, c * T:(c + 1) * T], stack(KA, KS, h, b, c), stack(QB, KS, h, b),
                              start=True, stop=True)
                last.then_inc(s.s1_done, 1)

            def turn_max(b):
                pe.wait_ge(s.mp_step, 4 * (b + 1))
                if b == 0:
                    pe.wait_ge(s.scb_ready, 1)
                else:
                    pe.wait_ge(s.mt_copied, b)
                for c in range(TC):
                    last = mm(MT[0:3 * NH, c * P:(c + 1) * P],
                              mpieces[:, b % 2, c, :, :].rearrange("p k h -> p (k h)"), identb[:, :],
                              start=True, stop=True)
                last.then_inc(s.mt_done, 1)

            def scores(u):
                b, h = u // NH, u % NH
                if u >= 2:
                    pe.wait_ge(s.exp_done, u - 1)
                elif u == 0:
                    pe.wait_ge(s.v_copied, NP)
                    pe.wait_ge(s.ones_in, 16 * NP)
                if u % (2 * NH) == 0:
                    pe.wait_ge(mask_in[b // 2], 32)
                if h == 0:
                    pe.wait_ge(mrow_in[b], 48)
                for c in range(TC):
                    last = mm(S2[u % 2][:, c * T:(c + 1) * T], stack(KA, KF, h, b, c), stack(QB, KF, h, b),
                              start=True, stop=True)
                last.then_inc(s.s2_done, 1)

            def context(u):
                b, h = u // NH, u % NH
                g, j = h // 4, h % 4
                pe.wait_ge(s.exp_done, u + 1)
                if u == 0:
                    pe.wait_ge(s.v_ones, 1)
                if h == 0 and b >= 1:
                    pe.wait_ge(s.c_copied, b)
                for c in range(TC):
                    last = mm(CX[32 * j:32 * j + 32, g * T:(g + 1) * T], V[:, b, c, h, :], E[:, u % NE, c, :],
                              start=(c == 0), stop=(c == TC - 1))
                last.then_inc(s.av_done, 1)

            def turn_context(b):
                pe.wait_ge(s.c_copied, b + 1)
                for g in range(2):
                    for c in range(TC):
                        n = g * TC + c
                        last = nc.tensor.transpose(CTB[:, n * P:(n + 1) * P], C[:, g, c * P:(c + 1) * P],
                                                   ident[:, :])
                last.then_inc(s.ct_done, 1)

            def turn_back(b):
                pe.wait_ge(s.cq_done, 4 * (b + 1))
                if b >= 1:
                    pe.wait_ge(s.xt_done, b)
                for c in range(TC):
                    last = nc.tensor.transpose(OW[:, c * P:(c + 1) * P], Cq[:, c, :], ident[:, :])
                last.then_inc(s.cqt_done, 1)

            def project_out(b):
                pe.wait_ge(s.cqt_copied, b + 1)
                if b == 0:
                    pe.wait_ge(s.ld_wo, 16)
                for c in range(TC):
                    last = mm(OW[:, T + c * P:T + (c + 1) * P], CqT[:, c * P:(c + 1) * P], wo[:, :],
                              start=True, stop=True)
                last.then_inc(s.wo_done, 1)

            for u in range(LEAD):
                scores_for_max(u)
                if u == 11:
                    turn_max(0)
            for u in range(NU):
                b, h = u // NH, u % NH
                scores(u)
                if u + LEAD < NU:
                    scores_for_max(u + LEAD)
                if u >= 2:
                    context(u - 2)
                if h == 3 and b + 1 < B:
                    turn_max(b + 1)
                if b >= 1:
                    if h == 3:
                        turn_context(b - 1)
                    if h == 4:
                        turn_back(b - 1)
                    if h == 6:
                        project_out(b - 1)
            context(NU - 2)
            context(NU - 1)
            turn_context(B - 1)
            turn_back(B - 1)
            project_out(B - 1)

            def seed(bank_, view, c, gate, k, first, x_cols):
                cols = slice(gate * T + c * P, gate * T + (c + 1) * P)
                mm(view, Wih[:, k, cols], XT[:, k, x_cols], start=first, stop=False, skip_group_check=True)

            def rz_view(bank_, c):
                return bank_[:, 0:SB * 2 * B].rearrange("p (s c b) -> p s c b", c=TC, b=B)[:, :, c, :]

            def n_view(bank_, c, slot):
                return bank_[:, 0:HB * G3].rearrange("p (s c b k) -> p s c b k", c=TC, b=B, k=3)[:, :, c, :, slot]

            def bias(view, row, c, steps):
                mm(view, bias3[:, row * T + c * P:row * T + (c + 1) * P], ones3[:, 0:steps * B],
                   start=False, stop=False, skip_group_check=True)

            def seed_rz(p, n, x_cols):
                gate, c, k = n // 4, (n // 2) % 2, n % 2
                bank_ = (R, Z)[gate][p]
                view = rz_view(bank_, c)
                seed(bank_, view, c, gate, k, c == 0 and k == 0, x_cols)
                if k == 1:
                    bias(view, gate, c, SB)

            def seed_n(hh, n, x_cols):
                c, k = n // 2, n % 2
                view = n_view(N[hh], c, 2)
                seed(N[hh], view, c, 2, k, c == 0 and k == 0, x_cols)
                if k == 1:
                    bias(view, 2, c, HB)
                    bias(n_view(N[hh], c, 0), 3, c, HB)

            pe.wait_ge(s.w_ready, 2)
            pe.wait_ge(s.bias_rows, 16)
            pe.wait_ge(s.zero_ready, 6)
            pe.wait_ge(s.xt_done, B)
            for n in range(8):
                seed_rz(0, n, slice(0, SB * B))
            for n in range(4):
                seed_n(0, n, slice(0, HB * B))

            def step(turn, t):
                p, st, hh, q = t // SB, t % SB, (t // HB) % 2, t % 2
                pair = h16[q][:, :].rearrange("p (c b k) -> p c b k", c=TC, k=3)

                def high(gate, lo, hi):
                    for n in range(lo, hi):
                        W, c, k = (Whi, Wlo)[n // 4], (n // 2) % 2, n % 2
                        last = mm((R, Z)[gate][p][:, 2 * B * st + c * B:2 * B * st + (c + 1) * B],
                                  W[:, k, gate * T + c * P:gate * T + (c + 1) * P], pair[:, k, :, 2],
                                  start=False, stop=False, skip_group_check=True)
                    return last

                def low(gate):
                    for n in range(4):
                        c, k = n // 2, n % 2
                        last = mm((R, Z)[gate][p][:, 2 * B * st + c * B:2 * B * st + (c + 1) * B],
                                  Whi[:, k, gate * T + c * P:gate * T + (c + 1) * P], pair[:, k, :, 1],
                                  start=False, stop=False, skip_group_check=True)
                    return last

                pe.wait_ge(s.high_ready, turn * BODY + t + 1)
                high(0, 0, 8)
                high(1, 0, 4)
                pe.wait_ge(s.low_ready, turn * BODY + t + 1)
                low(0).then_inc(s.r_done, 1)
                o = N[hh][:, G3 * (t % HB):G3 * (t % HB + 1)].rearrange("p (c b k) -> p c b k", c=TC, k=3)
                for n in range(8):
                    W, c, k = (Whi, Wlo)[n // 4], (n // 2) % 2, n % 2
                    last = mm(o[:, c, :, 0:2], W[:, k, 2 * T + c * P:2 * T + (c + 1) * P], pair[:, k, :, 1:3],
                              start=False, stop=False, skip_group_check=True)
                last.then_inc(s.scan1_in, 1)
                high(1, 4, 8)
                low(1).then_inc(s.z_done, 1)

            def turn_out(turn, p):
                pe.wait_ge(s.sum_done, turn * 4 + 2 * (p + 1))
                for c in range(TC):
                    last = nc.tensor.transpose(YT[:, c * P:(c + 1) * P], ysum[:, c, :], ident[:, :])
                last.then_inc(s.y_turned, 1)

            pe.wait_ge(s.w_ready, 2)
            def steps(turn, first=False):
                for t in range(BODY):
                    p, st = t // SB, t % SB
                    step(turn, t)
                    here = turn * (BODY * B) + p * SB * B
                    if st < HB and st % 2 == 0:
                        seed_n(1, st // 2, cols(here + HB * B, HB * B))
                    elif st >= HB and st % 2 == 0:
                        seed_n(0, (st - HB) // 2, cols(here + SB * B, HB * B))
                    else:
                        seed_rz(1 - p, st // 2, cols(here + SB * B, SB * B))
                    if t == 2 and not first:
                        turn_out(turn - 1, 1)
                    if t == SB + 2:
                        turn_out(turn, 0)

            steps(0, first=True)
            with pe.Fori(1, S // BODY) as turn:
                steps(turn)
            turn_out(S // BODY - 1, 1)

    return nc


def kernel(x, cond_2048, L0_cond_Wq, L0_cond_Wo, L1_cond_W_ih, L1_cond_W_hh, L1_cond_b_ih, L1_cond_b_hh):
    import numpy as np
    import concourse.bacc as bacc
    from concourse.bass_utils import run_bass_kernel_spmd

    x, cond = np.asarray(x), np.asarray(cond_2048)
    B, D, T = x.shape
    arrays = {
        "x": x,
        "x_t": x.transpose(2, 1, 0).reshape(T // 128, 128, D * B).transpose(1, 0, 2),
        "cond": cond,
        "h0_t": cond.T.reshape(T // 128, 128, B).transpose(1, 0, 2).reshape(128, -1),
        "wq_t": np.asarray(L0_cond_Wq).T,
        "wo_t": np.asarray(L0_cond_Wo).T,
        "w_ih": np.asarray(L1_cond_W_ih),
        "w_hh": np.asarray(L1_cond_W_hh),
        "b_ih": np.asarray(L1_cond_b_ih).reshape(1, -1),
        "b_hh": np.asarray(L1_cond_b_hh).reshape(1, -1),
    }
    arrays = {n: np.ascontiguousarray(a) for n, a in arrays.items()}
    nc = bacc.Bacc("TRN2", target_bir_lowering=False, num_devices=1)
    args = [nc.dram_tensor(n, a.shape, mybir.dt.from_np(a.dtype), kind="ExternalInput").ap()
            for n, a in arrays.items()]
    out = nc.dram_tensor("out", (B, D, T), mybir.dt.float32, kind="ExternalOutput").ap()
    attention_then_gru(nc, *args, out)
    result = run_bass_kernel_spmd(nc, [arrays], core_ids=[0])
    return result.results[0]["out"]
```

```python
import concourse.bass as bass
from concourse import mybir
from collections import namedtuple
from contextlib import ExitStack


def attention_then_gru(nc, x, x_t, cond, h0_t, wq_t, wo_t, w_ih, w_hh, b_ih, b_hh, out):
    fp32, bf16, fp16, i32 = mybir.dt.float32, mybir.dt.bfloat16, mybir.dt.float16, mybir.dt.int32
    ALU = mybir.AluOpType
    ACT = mybir.ActivationFunctionType
    AX = mybir.AxisListType

    B, D, T = x.shape
    NH = 8
    DK = D // NH
    P = 128
    TC = T // P
    NP = B // 2
    NU = B * NH
    NEG = -1e30
    HALF_SCALE = float(DK) ** -0.25
    KS = 6 * DK
    ROW_MASK, ROW_MAX = KS, KS + 1
    KF = ROW_MAX + 3
    LEAD = 15
    COPY_LAG, TURN_LAG, NORM_LAG, BACK_LAG, COPY_BACK_LAG, OUT_LAG, ADD_LAG = 11, 14, 15, 17, 18, 20, 21
    MAX_TURN = 3
    NE = 8
    GU = 4

    S = D
    SB = 16
    HB = SB // 2
    BODY = 2 * SB
    OUT_STEPS = (4, 8)
    G3 = 3 * TC * B
    UP = 64.0

    ctx = ExitStack()
    with ctx:
        def sb(name, shape, dt=fp32):
            return ctx.enter_context(nc.sbuf_tensor(name, shape, dt))

        def sem(name):
            return ctx.enter_context(nc.semaphore(name))

        X = sb("X", [P, B, T])
        XT = sb("XT", [P, TC, (S + SB) * B])
        maskb = sb("maskb", [P, B, T])
        wq = sb("wq", [P, D])
        wqp = sb("wqp", [P, D])
        wo = sb("wo", [P, D])
        mask8 = sb("mask8", [B, T])
        rows8 = sb("rows8", [B, 2, T], bf16)
        ident = sb("ident", [P, P])
        identb = sb("identb", [P, P], bf16)
        ones3 = sb("ones3", [3, 2 * T], bf16)
        onesf = sb("onesf", [1, P])
        qm = sb("qm", [P, 2, 2 * T])
        rest = sb("rest", [P, 2, 2 * T])
        pieces = sb("pieces", [P, NP, 3, 2 * T], bf16)
        KA = sb("KA", [P, NP, NH, 2, T], bf16)
        QB = sb("QB", [P, NP, NH, 2, T], bf16)
        V = sb("V", [P, B, TC, NH, 2 * DK])
        E = sb("E", [P, NE, TC, T])
        nmx = sb("nmx", [P, 2, TC, NH])
        mrest = sb("mrest", [P, TC, NH])
        mpieces = sb("mpieces", [P, 2, TC, 3, NH], bf16)
        mrows = sb("mrows", [3 * NH, 2, T], bf16)
        C = sb("C", [P, 2, T])
        rden = sb("rden", [P, TC, NH])
        Cq = sb("Cq", [P, TC, D])
        CqT = sb("CqT", [P, T])
        Wih = sb("Wih", [P, TC, 3 * T])
        Whh = sb("Whh", [P, TC, 3 * T])
        Whi = sb("Whi", [P, TC, 3 * T], fp16)
        Wlo = sb("Wlo", [P, TC, 3 * T], fp16)
        NB = 4 * TC
        bias_in = sb("bias_in", [NB, P])
        bias_rz = sb("bias_rz", [2 * TC, P])
        bpieces = sb("bpieces", [NB, 3, P], bf16)
        bias3 = sb("bias3", [3, 4 * T], bf16)
        wmax = sb("wmax", [P, TC])
        sc1 = sb("sc1", [1, 8])
        scb = sb("scb", [P, 3])
        h0 = sb("h0", [P, TC * B])
        gate_r = sb("gate_r", [P, G3])
        gate_warm = sb("gate_warm", [P, 1])
        gate_z = sb("gate_z", [P, G3])
        hs = sb("hs", [P, BODY, G3])
        h16 = [sb(f"h16_{i}", [P, G3], fp16) for i in range(2)]
        ysum = sb("ysum", [P, TC, SB * B])
        yout = sb("yout", [P, 2, T])

        bank = [ctx.enter_context(nc.psum_tensor(f"bank{i}", [P, 512], fp32)) for i in range(8)]
        S1, S2 = bank[0:2], (bank[2], bank[3], bank[7])
        NS2 = len(S2)
        CX, CTB, OW = bank[4], bank[5], bank[6]
        MT = CTB
        R, Z, N = (bank[0], bank[4]), (bank[1], bank[5]), (bank[2], bank[3])
        PRE, YT = bank[6], bank[7]

        rows_dram = nc.dram_tensor("mask_rows", [2, B, T], bf16, kind="Internal").ap()

        names = """ld_xt ld_m8 ld_wq ld_wo ld_whh ld_wih ld_bias ld_h0 const_ready rows_ready
            rows_stored ones_in bias_rows mask_in wqp_ready q_done v_done qm_done v_copied p1_done p2_done v_ones
            s1_done max_done mp_step mt_done mt_copied s2_done exp_done av_done c_copied ct_done
            rden_done cq_done cqt_done cqt_copied wo_done xt_done
            wmax_done wmax_row sc_step sc_bcast scb_ready w_step w_ready wih_ready b_step init_step
            zero_ready r_done z_done scan1_in pre_ready scan2_in high_ready h_ready low_ready
            sum_done y_turned y_copied""".split()
        s = namedtuple("Semaphores", names)(*[sem(n) for n in names])
        r1_done = [sem(f"r1_done{i}") for i in range(NP)]
        p3_done = [sem(f"p3_done{i}") for i in range(NP)]
        ld_x = [sem(f"ld_x{i}") for i in range(NP)]
        ld_mask = [sem(f"ld_mask{i}") for i in range(NP)]
        stack_in = [sem(f"stack_in{i}") for i in range(NP)]
        stack_in_pool = [sem(f"stack_in_pool{i}") for i in range(NP)]
        mrow_in = [sem(f"mrow_in{i}") for i in range(B)]

        y_free = [sem(f"y_free{i}") for i in range(2)]
        y_stored = [sem(f"y_stored{i}") for i in range(2)]

        block = ctx.enter_context(nc.Block())

        def cols(start, n):
            return slice(start, start + n) if isinstance(start, int) else bass.ds(start, n)

        def ahead(u, lag):
            return u >= lag and (u - lag) % NH == 0

        def b_of(u, lag):
            return (u - lag) // NH

        def s1_bank(u):
            return (S1[0], S1[1], CX)[u % 3] if u < LEAD - 2 else S1[u % 2]

        def s1_before(u):
            return max(w for w in range(u) if s1_bank(w) is s1_bank(u))

        def piece_ready(i, k):
            return ((s.p1_done, i + 1), (s.p2_done, i + 1), (p3_done[i], 1))[k]

        def stack_rows(stack, i, r):
            return stack[r * DK:(r + 1) * DK, i, :, :, :].rearrange("p h b t -> p (h b t)")

        def gate_cols(t):
            return slice(2 * B * t, 2 * B * (t + 1))

        @block.sync
        def _(sp):
            for i in range(NP):
                sp.dma_start(X[:, 2 * i:2 * i + 2, :], x[2 * i:2 * i + 2, :, :].rearrange("b d t -> d b t"))\
                    .then_inc(ld_x[i], 16)

            def fill_stacks(i, k):
                sp.wait_ge(*piece_ready(i, k))
                for stack, r in (((KA, 0), (KA, 3), (QB, 0), (QB, 1)), ((KA, 1), (QB, 3)), ((KA, 2),))[k]:
                    sp.dma_start(stack_rows(stack, i, r), pieces[:, i, k, :]).then_inc(stack_in[i], 16)

            def fill_max_rows(b):
                sp.wait_ge(s.mt_copied, b + 1)
                sp.dma_start(QB[ROW_MAX:ROW_MAX + 3, b // 2, :, b % 2, :], mrows[:, b % 2, :])\
                    .then_inc(mrow_in[b], 16)

            for i in range(2):
                for k in range(3):
                    fill_stacks(i, k)
            sp.wait_ge(s.const_ready, 6)
            sp.dma_start(KA[ROW_MAX:ROW_MAX + 3, :, :, :, :].rearrange("p i h b t -> p (i h) (b t)"),
                         ones3[:, :].unsqueeze(1).to_broadcast([3, NP * NH, 2 * T])).then_inc(s.ones_in, 16)
            sp.wait_ge(s.rows_stored, 16)
            for r, stack in ((0, KA), (1, QB)):
                sp.dma_start(stack[ROW_MASK:ROW_MASK + 1, :, :, :, :].rearrange("p i h b t -> p i h (b t)"),
                             rows_dram[r:r + 1, :, :].rearrange("r (i b) t -> r i (b t)", b=2)
                             .unsqueeze(2).to_broadcast([1, NP, NH, 2 * T])).then_inc(s.mask_in, 16)
            sp.dma_start(Whh[:, :, :], w_hh.rearrange("(c p) n -> p c n", p=P)).then_inc(s.ld_whh, 16)
            fill_max_rows(0)
            for k in range(3):
                fill_stacks(2, k)
            sp.dma_start(bias_in[0:3 * TC, :], b_ih).then_inc(s.ld_bias, 16)
            sp.dma_start(bias_in[3 * TC:4 * TC, :], b_hh[2 * TC:3 * TC, :]).then_inc(s.ld_bias, 16)
            sp.dma_start(bias_rz[:, :], b_hh[0:2 * TC, :]).then_inc(s.ld_bias, 16)
            sp.dma_start(wo[:, :], wo_t).then_inc(s.ld_wo, 16)
            fill_max_rows(1)
            sp.dma_start(XT[:, :, 0:S * B], x_t).then_inc(s.ld_xt, 16)
            for k in range(3):
                fill_stacks(3, k)
            fill_max_rows(2)
            sp.dma_start(Wih[:, :, :], w_ih.rearrange("(c p) n -> p c n", p=P)).then_inc(s.ld_wih, 16)
            sp.dma_start(h0[:, :], h0_t).then_inc(s.ld_h0, 16)
            fill_max_rows(3)
            sp.wait_ge(s.b_step, 6)
            for k in range(3):
                sp.dma_start(bias3[k:k + 1, :], bpieces[:, k, :]).then_inc(s.bias_rows, 16)
            for b in range(4, B):
                fill_max_rows(b)
            for p in range(2):
                sp.sem_inc(y_free[p], 1)
            with sp.Fori(0, S // BODY) as turn:
                for p in range(2):
                    sp.wait_ge(s.y_copied, turn * 2 + p + 1)
                    sp.dma_start(out[:, bass.ds(turn * BODY + p * SB, SB), :].rearrange("b t f -> t b f"),
                                 yout[:, p, :]).then_inc(y_stored[p], 16)
                    sp.wait_ge(y_stored[p], turn * 16 + 16)
                    sp.sem_inc(y_free[p], 1)

        @block.gpsimd
        def _(pool):
            pool.memset(ident[:, :], 0.0).then_inc(s.const_ready, 1)
            pool.memset(identb[:, :], 0.0).then_inc(s.const_ready, 1)
            pool.memset(ones3[:, :], 1.0).then_inc(s.const_ready, 1)
            pool.memset(onesf[:, :], 1.0).then_inc(s.const_ready, 1)
            pool.wait_ge(s.const_ready, 4)
            for m in (ident, identb):
                pool.affine_select(out=m[:, :], in_=m[:, :], compare_op=ALU.not_equal, fill=1.0, base=0,
                                   pattern=[[-1, P]], channel_multiplier=1).then_inc(s.const_ready, 1)
            pool.memset(V[:, :, :, :, DK:2 * DK].rearrange("p b c h k -> p (b c h) k"), 1.0).then_inc(s.v_ones, 1)
            pool.wait_ge(s.ld_m8, 16)
            pool.tensor_scalar(rows8[:, 0, :], mask8[:, :], -1.0, 1.0, ALU.mult, ALU.add).then_inc(s.rows_ready, 1)
            pool.tensor_scalar(rows8[:, 1, :], mask8[:, :], NEG, None, ALU.mult).then_inc(s.rows_ready, 1)

            def fill_stacks(i, k):
                pool.wait_ge(*piece_ready(i, k))
                for stack, r in (((KA, 5), (QB, 2)), ((KA, 4), (QB, 4)), ((QB, 5),))[k]:
                    pool.dma_start(stack_rows(stack, i, r), pieces[:, i, k, :]).then_inc(stack_in_pool[i], 16)

            for k in range(3):
                fill_stacks(0, k)
            pool.wait_ge(s.rows_ready, 2)
            pool.dma_start(rows_dram.rearrange("r b t -> b r t"), rows8[:, :, :]).then_inc(s.rows_stored, 16)
            for k in range(3):
                fill_stacks(1, k)

            def max_pieces(b):
                j = b % 2
                pool.wait_ge(s.max_done, NH * (b + 1))
                if b >= 2:
                    pool.wait_ge(s.mt_done, b - 1)
                n = 4 * b
                pool.tensor_copy(mpieces[:, j, :, 0, :], nmx[:, j, :, :]).then_inc(s.mp_step, 1)
                pool.wait_ge(s.mp_step, n + 1)
                pool.tensor_tensor(mrest[:, :, :], nmx[:, j, :, :], mpieces[:, j, :, 0, :],
                                   ALU.subtract).then_inc(s.mp_step, 1)
                pool.wait_ge(s.mp_step, n + 2)
                pool.tensor_copy(mpieces[:, j, :, 1, :], mrest[:, :, :]).then_inc(s.mp_step, 1)
                pool.wait_ge(s.mp_step, n + 3)
                pool.tensor_tensor(mpieces[:, j, :, 2, :], mrest[:, :, :], mpieces[:, j, :, 1, :],
                                   ALU.subtract).then_inc(s.mp_step, 1)

            def whh_pieces(gate):
                cols = slice(gate * T, (gate + 1) * T)
                if gate == 0:
                    pool.wait_ge(s.scb_ready, 1)
                pool.tensor_scalar(Whh[:, :, cols], Whh[:, :, cols], scb[:, 2:3], None, ALU.mult)\
                    .then_inc(s.w_step, 1)
                pool.wait_ge(s.w_step, 2 * gate + 1)
                pool.tensor_copy(Whi[:, :, cols], Whh[:, :, cols]).then_inc(s.w_step, 1)
                pool.wait_ge(s.w_step, 2 * gate + 2)
                pool.tensor_tensor(Wlo[:, :, cols], Whh[:, :, cols], Whi[:, :, cols], ALU.subtract)\
                    .then_inc(s.w_ready, 1)

            def bias_pieces():
                pool.wait_ge(s.ld_bias, 48)
                pool.tensor_tensor(bias_in[0:2 * TC, :], bias_in[0:2 * TC, :], bias_rz[:, :], ALU.add)\
                    .then_inc(s.b_step, 1)
                pool.wait_ge(s.b_step, 1)
                pool.tensor_scalar(bias_in[:, :], bias_in[:, :], UP, None, ALU.mult).then_inc(s.b_step, 1)
                pool.wait_ge(s.b_step, 2)
                pool.tensor_copy(bpieces[:, 0, :], bias_in[:, :]).then_inc(s.b_step, 1)
                pool.wait_ge(s.b_step, 3)
                pool.tensor_tensor(bias_in[:, :], bias_in[:, :], bpieces[:, 0, :], ALU.subtract).then_inc(s.b_step, 1)
                pool.wait_ge(s.b_step, 4)
                pool.tensor_copy(bpieces[:, 1, :], bias_in[:, :]).then_inc(s.b_step, 1)
                pool.wait_ge(s.b_step, 5)
                pool.tensor_tensor(bpieces[:, 2, :], bias_in[:, :], bpieces[:, 1, :], ALU.subtract)\
                    .then_inc(s.b_step, 1)

            def gru_start():
                pool.memset(XT[:, :, S * B:(S + SB) * B], 0.0).then_inc(s.zero_ready, 1)
                pool.memset(gate_r[:, 0::3], 0.0).then_inc(s.zero_ready, 1)
                pool.memset(gate_r[:, 1::3], 1.0).then_inc(s.zero_ready, 1)
                pool.memset(gate_z[:, 0::3], 0.0).then_inc(s.zero_ready, 1)
                pool.memset(gate_z[:, 1::3], 1.0).then_inc(s.zero_ready, 1)
                pool.memset(hs[:, BODY - 1, 0::3], 0.0).then_inc(s.zero_ready, 1)
                pool.wait_ge(s.zero_ready, 6)
                pool.wait_ge(s.scb_ready, 1)
                pool.tensor_scalar(gate_z[:, 1::3], gate_z[:, 1::3], scb[:, 0:1], None,
                                   ALU.mult).then_inc(s.zero_ready, 1)
                pool.wait_ge(s.ld_h0, 16)
                pool.tensor_scalar(hs[:, BODY - 1, 2::3], h0[:, :], scb[:, 0:1], None,
                                   ALU.mult).then_inc(s.init_step, 1)
                pool.wait_ge(s.init_step, 1)
                pool.tensor_scalar(hs[:, BODY - 1, 1::3], hs[:, BODY - 1, 2::3], -1.0, None,
                                   ALU.mult).then_inc(s.scan2_in, 1)
                pool.tensor_copy(h16[0][:, 2::3], hs[:, BODY - 1, 2::3]).then_inc(s.high_ready, 1)
                pool.wait_ge(s.high_ready, 1)
                pool.tensor_tensor(h16[0][:, 1::3], hs[:, BODY - 1, 2::3], h16[0][:, 2::3],
                                   ALU.subtract).then_inc(s.low_ready, 1)

            for b in range(B):
                max_pieces(b)
                if b < 2:
                    for k in range(3):
                        fill_stacks(b + 2, k)
                if b == 2:
                    bias_pieces()
                elif 3 <= b < 6:
                    whh_pieces(b - 3)
            gru_start()

        @block.scalar
        def _(act):
            act.dma_start(wq[:, :], wq_t).then_inc(s.ld_wq, 16)
            for i in range(NP):
                act.dma_start(maskb[:, 2 * i:2 * i + 2, :].rearrange("p b t -> p (b t)"),
                              cond[2 * i:2 * i + 2, :].rearrange("(o b) t -> o (b t)", o=1)
                              .to_broadcast([P, 2 * T])).then_inc(ld_mask[i], 16)
                if i == 0:
                    act.dma_start(mask8[:, :], cond).then_inc(s.ld_m8, 16)

            def piece_1(i):
                act.wait_ge(s.qm_done, i + 1)
                nc.scalar.activation(pieces[:, i, 0, :], qm[:, i % 2, :], ACT.Copy).then_inc(s.p1_done, 1)

            def piece_2(i):
                act.wait_ge(r1_done[i], 1)
                nc.scalar.activation(pieces[:, i, 1, :], rest[:, i % 2, :], ACT.Copy).then_inc(s.p2_done, 1)

            def copy_v(i):
                act.wait_ge(s.v_done, i + 1)
                nc.scalar.activation(V[:, 2 * i:2 * i + 2, :, :, 0:DK].rearrange("p b c h k -> p (b c h) k"),
                                     S2[i % 2][:, :].rearrange("p (n k) -> p n k", k=DK), ACT.Copy)\
                    .then_inc(s.v_copied, 1)

            def wih_scaled(k):
                act.wait_ge(s.ld_wih, 16)
                nc.scalar.activation(Wih[:, k, :], Wih[:, k, :], ACT.Copy, scale=UP).then_inc(s.wih_ready, 1)

            piece_1(0)
            piece_2(0)
            copy_v(0)
            for i in range(1, NP):
                piece_1(i)
                copy_v(i)
                if i < NP - 1:
                    piece_2(i)

            def copy_max(b):
                act.wait_ge(s.mt_done, b + 1)
                if b >= 2:
                    act.wait_ge(mrow_in[b - 2], 16)
                nc.scalar.activation(mrows[:, b % 2, :], MT[0:3 * NH, 0:T], ACT.Copy).then_inc(s.mt_copied, 1)

            def copy_context(b):
                act.wait_ge(s.av_done, 2 * (b + 1))
                nc.scalar.activation(C[:, :, :].rearrange("p g t -> p (g t)"), CX[:, :], ACT.Copy)\
                    .then_inc(s.c_copied, 1)

            def copy_turned(b):
                act.wait_ge(s.cqt_done, b + 1)
                nc.scalar.activation(CqT[:, :], OW[:, 0:T], ACT.Copy).then_inc(s.cqt_copied, 1)

            copy_max(0)
            for u in range(NU):
                b, h = u // NH, u % NH
                act.wait_ge(s.s2_done, u + 1)
                if u >= NE and u % GU == 0:
                    act.wait_ge(s.av_done, (u - NE) // GU + 1)
                nc.scalar.activation(E[:, u % NE, :, :].rearrange("p c t -> p (c t)"), S2[u % NS2][:, :], ACT.Exp)\
                    .then_inc(s.exp_done, 1)
                if u == 1:
                    piece_2(NP - 1)
                if h == MAX_TURN and b + 1 < B:
                    copy_max(b + 1)
                if h == 6 and 3 <= b < 3 + TC:
                    wih_scaled(b - 3)
                if ahead(u, COPY_LAG):
                    copy_context(b_of(u, COPY_LAG))
                if ahead(u, COPY_BACK_LAG):
                    copy_turned(b_of(u, COPY_BACK_LAG))
            copy_turned(B - 2)
            copy_context(B - 1)
            nc.scalar.activation(gate_warm[:, :], ident[:, 0:1], ACT.Sigmoid)
            copy_turned(B - 1)

            def copy_out(turn, p):
                act.wait_ge(y_free[p], turn + 1)
                act.wait_ge(s.y_turned, TC * (turn * 2 + p + 1))
                nc.scalar.activation(yout[:, p, :], YT[:, 0:TC * P], ACT.Copy).then_inc(s.y_copied, 1)

            def gates(turn, first=False):
                for t in range(BODY):
                    p, st = t // SB, t % SB
                    act.wait_ge(s.r_done, turn * BODY + t + 1)
                    nc.scalar.activation(gate_r[:, 2::3], R[p][:, gate_cols(st)], ACT.Sigmoid, scale=1.0 / UP)\
                        .then_inc(s.scan1_in, 1)
                    act.wait_ge(s.z_done, turn * BODY + t + 1)
                    nc.scalar.activation(gate_z[:, 2::3], Z[p][:, gate_cols(st)], ACT.Sigmoid, scale=-1.0 / UP)\
                        .then_inc(s.scan2_in, 1)
                    act.wait_ge(s.pre_ready, turn * BODY + t + 1)
                    nc.scalar.activation(hs[:, (t - 1) % BODY, 0::3], PRE[:, 2:G3:3], ACT.Tanh, scale=1.0 / UP)\
                        .then_inc(s.scan2_in, 1)
                    if t == OUT_STEPS[-1] + 1 and not first:
                        copy_out(turn - 1, 1)
                    if t == SB + OUT_STEPS[-1] + 1:
                        copy_out(turn, 0)

            gates(0, first=True)
            with act.Fori(1, S // BODY) as turn:
                gates(turn)
            copy_out(S // BODY - 1, 1)

        @block.vector
        def _(dve):
            dve.wait_ge(s.ld_wq, 16)
            nc.vector.tensor_copy(wqp[:, :].rearrange("d (k h) -> d k h", h=NH),
                                  wq[:, :].rearrange("d (h k) -> d k h", k=DK)).then_inc(s.wqp_ready, 1)
            def masked_q(i):
                dve.wait_ge(ld_mask[i], 16)
                dve.wait_ge(s.q_done, i + 1)
                nc.vector.scalar_tensor_tensor(
                    qm[:, i % 2, :], S1[i % 2][:, :], HALF_SCALE,
                    maskb[:, 2 * i:2 * i + 2, :].rearrange("p b t -> p (b t)"), ALU.mult, ALU.mult)\
                    .then_inc(s.qm_done, 1)

            def rest_1(i):
                dve.wait_ge(s.p1_done, i + 1)
                nc.vector.tensor_tensor(rest[:, i % 2, :], qm[:, i % 2, :], pieces[:, i, 0, :], ALU.subtract)\
                    .then_inc(r1_done[i], 1)

            def piece_3(i):
                dve.wait_ge(s.p2_done, i + 1)
                nc.vector.tensor_tensor(pieces[:, i, 2, :], rest[:, i % 2, :], pieces[:, i, 1, :], ALU.subtract)\
                    .then_inc(p3_done[i], 1)

            masked_q(0)
            rest_1(0)
            for i in range(1, NP):
                masked_q(i)
                piece_3(i - 1)
                if i < NP - 1:
                    rest_1(i)

            def weight_max(c):
                if c == 0:
                    dve.wait_ge(s.ld_whh, 16)
                nc.vector.reduce_max(wmax[:, c:c + 1], Whh[:, c, :], AX.X,
                                     apply_absolute_value=True).then_inc(s.wmax_done, 1)

            def scale_step(n):
                if n == 0:
                    dve.wait_ge(s.wmax_row, 1)
                    nc.vector.reduce_max(sc1[:, 0:1], OW[0:1, 0:TC * P], AX.X).then_inc(s.sc_step, 1)
                    return
                dve.wait_ge(s.sc_step, n)
                if n == 1:
                    nc.vector.tensor_single_scalar(sc1[:, 1:2].bitcast(i32), sc1[:, 0:1].bitcast(i32), 0x7F800000,
                                                   ALU.bitwise_and).then_inc(s.sc_step, 1)
                elif n == 2:
                    nc.vector.tensor_scalar(sc1[:, 2:3], sc1[:, 1:2], 2.0 ** -8, 1.0, ALU.mult, ALU.max)\
                        .then_inc(s.sc_step, 1)
                elif n == 3:
                    nc.vector.tensor_scalar(sc1[:, 4:5], sc1[:, 2:3], 2.0 ** 15, None, ALU.min)\
                        .then_inc(s.sc_step, 1)
                elif n == 4:
                    nc.vector.reciprocal(sc1[:, 5:6], sc1[:, 4:5]).then_inc(s.sc_step, 1)
                elif n == 5:
                    nc.vector.tensor_scalar(sc1[:, 6:7], sc1[:, 5:6], UP, None, ALU.mult).then_inc(s.sc_step, 1)

            def scales_out():
                dve.wait_ge(s.sc_bcast, 1)
                nc.vector.tensor_copy(scb[:, :], OW[:, 0:3]).then_inc(s.scb_ready, 1)

            def row_max(u):
                b, h = u // NH, u % NH
                dve.wait_ge(s.s1_done, u + 1)
                if b >= 2 and h == 0:
                    dve.wait_ge(s.mp_step, 4 * (b - 1))
                nc.vector.reduce_max(nmx[:, b % 2, :, h], s1_bank(u)[:, :].rearrange("p (c t) -> p c t", c=TC),
                                     AX.X, negate=True).then_inc(s.max_done, 1)

            def normalise(b):
                turned = CTB[:, :].rearrange("p (c h k) -> p c h k", c=TC, k=2 * DK)
                dve.wait_ge(s.ct_done, b + 1)
                nc.vector.reciprocal(rden[:, :, :], turned[:, :, :, DK]).then_inc(s.rden_done, 1)
                dve.wait_ge(s.rden_done, b + 1)
                if b >= 1:
                    dve.wait_ge(s.cqt_done, b)
                nc.vector.tensor_tensor(Cq[:, :, :].rearrange("p c (h k) -> p c h k", k=DK),
                                        turned[:, :, :, 0:DK],
                                        rden[:, :, :].unsqueeze(3).to_broadcast([P, TC, NH, DK]),
                                        ALU.mult).then_inc(s.cq_done, 1)

            def add_residual(b):
                dve.wait_ge(s.wo_done, b + 1)
                xb = XT[:, :, b:S * B:B]
                nc.vector.tensor_tensor(xb, OW[:, T:2 * T].rearrange("p (c d) -> p c d", c=TC), xb, ALU.add)\
                    .then_inc(s.xt_done, 1)

            for u in range(LEAD):
                row_max(u)
            for u in range(NU):
                b, h = u // NH, u % NH
                if u + LEAD < NU:
                    row_max(u + LEAD)
                if u == 0:
                    rest_1(NP - 1)
                if u == 3:
                    piece_3(NP - 1)
                if u in (4, 6):
                    weight_max((4, 6).index(u))
                if 9 <= u < 15:
                    scale_step(u - 9)
                if u == 15:
                    scales_out()
                if u == 18:
                    dve.wait_ge(s.ld_xt, 16)
                if ahead(u, NORM_LAG):
                    normalise(b_of(u, NORM_LAG))
                if ahead(u, ADD_LAG):
                    add_residual(b_of(u, ADD_LAG))
            add_residual(B - 2)
            normalise(B - 1)
            add_residual(B - 1)

            dve.wait_ge(s.zero_ready, 7)

            def sum_block(turn, p, c):
                if c == 0:
                    dve.wait_ge(s.h_ready, turn * BODY + SB * (p + 1))
                src = hs[:, SB * p:SB * (p + 1), 24 * c + 2:24 * c + 24:3]
                xx = XT[:, c, cols(turn * (BODY * B) + p * SB * B, SB * B)]
                nc.vector.scalar_tensor_tensor(ysum[:, c, :].rearrange("p (s b) -> p s b", b=B), src, scb[:, 1:2],
                                               xx.rearrange("p (s b) -> p s b", b=B), ALU.mult, ALU.add)\
                    .then_inc(s.sum_done, 1)

            def scans(turn, first=False):
                for t in range(BODY):
                    hh = (t // HB) % 2
                    dve.wait_ge(s.scan1_in, turn * (2 * BODY) + 2 * (t + 1))
                    nc.vector.tensor_tensor_scan(PRE[:, 0:G3], gate_r[:, :],
                                                 N[hh][:, G3 * (t % HB):G3 * (t % HB + 1)], 0.0,
                                                 ALU.mult, ALU.add).then_inc(s.pre_ready, 1)
                    dve.wait_ge(s.scan2_in, turn * (3 * BODY) + 3 * (t + 1))
                    before = hs[:, (t - 1) % BODY, :]
                    nc.vector.tensor_tensor_scan(h16[(t + 1) % 2][:, :], gate_z[:, :], before, 0.0,
                                                 ALU.mult, ALU.add).then_inc(s.high_ready, 1)
                    nc.vector.tensor_tensor_scan(hs[:, t, :], gate_z[:, :], before, 0.0,
                                                 ALU.mult, ALU.add).then_inc(s.h_ready, 1)
                    dve.wait_ge(s.h_ready, turn * BODY + t + 1)
                    nc.vector.tensor_tensor(h16[(t + 1) % 2][:, 1::3], hs[:, t, 2::3], h16[(t + 1) % 2][:, 2::3],
                                            ALU.subtract).then_inc(s.low_ready, 1)
                    nc.vector.tensor_scalar(hs[:, t, 1::3], hs[:, t, 2::3], -1.0, None, ALU.mult)\
                        .then_inc(s.scan2_in, 1)
                    if t < TC and not first:
                        sum_block(turn - 1, 1, t)
                    if SB <= t < SB + TC:
                        sum_block(turn, 0, t - SB)

            scans(0, first=True)
            with dve.Fori(1, S // BODY) as turn:
                scans(turn)
            for c in range(TC):
                sum_block(S // BODY - 1, 1, c)

        @block.tensor
        def _(pe):
            mm = nc.tensor.matmul
            pe.wait_ge(s.ld_wq, 16)
            pe.wait_ge(s.wqp_ready, 1)

            def project_q(i):
                pe.wait_ge(ld_x[i], 16)
                if i >= 2:
                    pe.wait_ge(s.qm_done, i - 1)
                mm(S1[i % 2][:, :], wqp[:, :],
                   X[:, 2 * i:2 * i + 2, :].rearrange("d b t -> d (b t)"), start=True, stop=True)\
                    .then_inc(s.q_done, 1)

            def project_v(i):
                if i >= 2:
                    pe.wait_ge(s.v_copied, i - 1)
                for n in range(2 * TC):
                    b, c = 2 * i + n // TC, n % TC
                    last = mm(S2[i % 2][:, n * P:(n + 1) * P], X[:, b, c * P:(c + 1) * P], wq[:, :],
                              start=True, stop=True)
                last.then_inc(s.v_done, 1)

            project_q(0)
            project_q(1)
            project_v(0)
            project_q(2)
            project_v(1)
            project_q(3)
            project_v(2)
            project_v(3)

            def weight_max_row():
                pe.wait_ge(s.wmax_done, TC)
                for c in range(TC):
                    last = mm(OW[0:1, c * P:(c + 1) * P], wmax[:, c:c + 1], ident[:, :],
                              start=True, stop=True)
                last.then_inc(s.wmax_row, 1)

            def scales_to_all():
                pe.wait_ge(s.sc_step, 6)
                mm(OW[:, 0:3], onesf[:, :], sc1[:, 4:7], start=True, stop=True).then_inc(s.sc_bcast, 1)

            def stack(tile, rows, h, b, c=None):
                cols = slice(0, T) if c is None else slice(c * P, (c + 1) * P)
                return tile[0:rows, b // 2, h, b % 2, cols]

            def scores_for_max(u):
                b, h = u // NH, u % NH
                if u < 3:
                    pe.wait_ge(s.qm_done, NP)
                else:
                    pe.wait_ge(s.max_done, s1_before(u) + 1)
                if u % (2 * NH) == 0:
                    pe.wait_ge(stack_in[b // 2], 16 * 7)
                    pe.wait_ge(stack_in_pool[b // 2], 16 * 5)
                for c in range(TC):
                    last = mm(s1_bank(u)[:, c * T:(c + 1) * T], stack(KA, KS, h, b, c), stack(QB, KS, h, b),
                              start=True, stop=True)
                last.then_inc(s.s1_done, 1)

            def turn_max(b):
                pe.wait_ge(s.mp_step, 4 * (b + 1))
                if b == 0:
                    pe.wait_ge(s.const_ready, 6)
                if b >= 3:
                    pe.wait_ge(s.cq_done, b - 2)
                for c in range(TC):
                    last = mm(MT[0:3 * NH, c * P:(c + 1) * P],
                              mpieces[:, b % 2, c, :, :].rearrange("p k h -> p (k h)"), identb[:, :],
                              start=True, stop=True)
                last.then_inc(s.mt_done, 1)

            def scores(u):
                b, h = u // NH, u % NH
                if u >= NS2:
                    pe.wait_ge(s.exp_done, u - NS2 + 1)
                elif u == 0:
                    pe.wait_ge(s.v_copied, NP)
                    pe.wait_ge(s.ones_in, 16)
                    pe.wait_ge(s.mask_in, 32)
                if h == 0:
                    pe.wait_ge(mrow_in[b], 16)
                for c in range(TC):
                    last = mm(S2[u % NS2][:, c * T:(c + 1) * T], stack(KA, KF, h, b, c), stack(QB, KF, h, b),
                              start=True, stop=True)
                last.then_inc(s.s2_done, 1)

            def context(g, c):
                b = g * GU // NH
                if c == 0:
                    pe.wait_ge(s.exp_done, GU * (g + 1))
                if g == 0:
                    pe.wait_ge(s.v_ones, 1)
                    pe.wait_ge(s.max_done, LEAD - 2)
                if g % 2 == 0 and b >= 1:
                    pe.wait_ge(s.c_copied, b)
                for j in range(GU):
                    u = g * GU + j
                    last = mm(CX[32 * j:32 * j + 32, (g % 2) * T:(g % 2 + 1) * T], V[:, b, c, u % NH, :],
                              E[:, u % NE, c, :], start=(c == 0), stop=(c == TC - 1), skip_group_check=True)
                if c == TC - 1:
                    last.then_inc(s.av_done, 1)

            def turn_context(b):
                pe.wait_ge(s.c_copied, b + 1)
                pe.wait_ge(s.mt_copied, min(b + 3, B))
                if b >= 1:
                    pe.wait_ge(s.cq_done, b)
                for c in range(TC):
                    for g in range(2):
                        n = c * 2 + g
                        last = nc.tensor.transpose(CTB[:, n * P:(n + 1) * P], C[:, g, c * P:(c + 1) * P],
                                                   ident[:, :])
                last.then_inc(s.ct_done, 1)

            def turn_back(b):
                pe.wait_ge(s.cq_done, b + 1)
                if b == 0:
                    pe.wait_ge(s.scb_ready, 1)
                else:
                    pe.wait_ge(s.xt_done, b)
                for c in range(TC):
                    last = nc.tensor.transpose(OW[:, c * P:(c + 1) * P], Cq[:, c, :], ident[:, :])
                last.then_inc(s.cqt_done, 1)

            def project_out(b):
                pe.wait_ge(s.cqt_copied, b + 1)
                if b == 0:
                    pe.wait_ge(s.ld_wo, 16)
                for c in range(TC):
                    last = mm(OW[:, T + c * P:T + (c + 1) * P], CqT[:, c * P:(c + 1) * P], wo[:, :],
                              start=True, stop=True)
                last.then_inc(s.wo_done, 1)

            def seed(view, c, gate, k, first, xs):
                cols = slice(gate * T + c * P, gate * T + (c + 1) * P)
                mm(view, Wih[:, k, cols], xs, start=first, stop=False, skip_group_check=True)

            def rz_view(bank_, c):
                return bank_[:, 0:SB * 2 * B].rearrange("p (s c b) -> p s c b", c=TC, b=B)[:, :, c, :]

            def n_view(bank_, c, slot):
                return bank_[:, 0:HB * G3].rearrange("p (s c b k) -> p s c b k", c=TC, b=B, k=3)[:, :, c, :, slot]

            def bias(view, row, c, steps):
                mm(view, bias3[:, row * T + c * P:row * T + (c + 1) * P], ones3[:, 0:steps * B],
                   start=False, stop=False, skip_group_check=True)

            def seed_rz(p, n, x_cols):
                gate, c, k = n // 4, (n // 2) % 2, n % 2
                bank_ = (R, Z)[gate][p]
                view = rz_view(bank_, c)
                seed(view, c, gate, k, c == 0 and k == 0, XT[:, k, x_cols])
                if k == 1:
                    bias(view, gate, c, SB)

            def seed_n(hh, n, x_cols):
                c, k = n // 2, n % 2
                view = n_view(N[hh], c, 2)
                seed(view, c, 2, k, c == 0 and k == 0, XT[:, k, x_cols])
                if k == 1:
                    bias(view, 2, c, HB)
                    bias(n_view(N[hh], c, 0), 3, c, HB)

            for u in range(LEAD):
                scores_for_max(u)
                if u == NH + 3:
                    turn_max(0)
            for u in range(NU):
                b, h = u // NH, u % NH
                scores(u)
                if u + LEAD < NU:
                    scores_for_max(u + LEAD)
                if u >= GU and u % GU == 1:
                    context((u - GU) // GU, 0)
                if u >= GU and u % GU == 2:
                    context((u - GU) // GU, 1)
                if h == MAX_TURN and b + 1 < B:
                    turn_max(b + 1)
                if u == 8:
                    weight_max_row()
                if u == 15:
                    scales_to_all()
                if ahead(u, TURN_LAG):
                    turn_context(b_of(u, TURN_LAG))
                if ahead(u, BACK_LAG):
                    turn_back(b_of(u, BACK_LAG))
                if ahead(u, OUT_LAG):
                    project_out(b_of(u, OUT_LAG))
            turn_back(B - 2)
            context(NU // GU - 1, 0)
            context(NU // GU - 1, 1)
            project_out(B - 2)
            turn_context(B - 1)
            turn_back(B - 1)
            project_out(B - 1)

            pe.wait_ge(s.wih_ready, TC)
            pe.wait_ge(s.bias_rows, 48)
            pe.wait_ge(s.xt_done, B)
            for n in range(4):
                seed_rz(0, n, slice(0, SB * B))
            for n in range(4):
                seed_n(0, n, slice(0, HB * B))
            for n in range(4, 8):
                seed_rz(0, n, slice(0, SB * B))
            pe.wait_ge(s.w_ready, 3)
            pe.wait_ge(s.zero_ready, 6)

            def step(turn, t):
                p, st, hh, q = t // SB, t % SB, (t // HB) % 2, t % 2
                pair = h16[q][:, :].rearrange("p (c b k) -> p c b k", c=TC, k=3)

                def high(gate, lo, hi):
                    for n in range(lo, hi):
                        W, c, k = (Whi, Wlo)[n // 4], (n // 2) % 2, n % 2
                        last = mm((R, Z)[gate][p][:, 2 * B * st + c * B:2 * B * st + (c + 1) * B],
                                  W[:, k, gate * T + c * P:gate * T + (c + 1) * P], pair[:, k, :, 2],
                                  start=False, stop=False, skip_group_check=True)
                    return last

                def low(gate):
                    for n in range(4):
                        c, k = n // 2, n % 2
                        last = mm((R, Z)[gate][p][:, 2 * B * st + c * B:2 * B * st + (c + 1) * B],
                                  Whi[:, k, gate * T + c * P:gate * T + (c + 1) * P], pair[:, k, :, 1],
                                  start=False, stop=False, skip_group_check=True)
                    return last

                pe.wait_ge(s.high_ready, turn * BODY + t + 1)
                high(0, 0, 8)
                high(1, 0, 5)
                pe.wait_ge(s.low_ready, turn * BODY + t + 1)
                low(0).then_inc(s.r_done, 1)
                o = N[hh][:, G3 * (t % HB):G3 * (t % HB + 1)].rearrange("p (c b k) -> p c b k", c=TC, k=3)
                for n in range(8):
                    W, c, k = (Whi, Wlo)[n // 4], (n // 2) % 2, n % 2
                    last = mm(o[:, c, :, 0:2], W[:, k, 2 * T + c * P:2 * T + (c + 1) * P], pair[:, k, :, 1:3],
                              start=False, stop=False, skip_group_check=True)
                last.then_inc(s.scan1_in, 1)
                high(1, 5, 8)
                low(1).then_inc(s.z_done, 1)

            def turn_out(turn, p, c):
                pe.wait_ge(s.sum_done, turn * (2 * TC) + TC * p + c + 1)
                nc.tensor.transpose(YT[:, c * P:(c + 1) * P], ysum[:, c, :], ident[:, :]).then_inc(s.y_turned, 1)

            def steps(turn, first=False):
                for t in range(BODY):
                    p, st = t // SB, t % SB
                    step(turn, t)
                    here = turn * (BODY * B) + p * SB * B
                    if st < HB and st % 2 == 0:
                        seed_n(1, st // 2, cols(here + HB * B, HB * B))
                    elif st >= HB and st % 2 == 0:
                        seed_n(0, (st - HB) // 2, cols(here + SB * B, HB * B))
                    else:
                        seed_rz(1 - p, st // 2, cols(here + SB * B, SB * B))
                    if t in OUT_STEPS and not first:
                        turn_out(turn - 1, 1, OUT_STEPS.index(t))
                    if t - SB in OUT_STEPS:
                        turn_out(turn, 0, OUT_STEPS.index(t - SB))

            steps(0, first=True)
            with pe.Fori(1, S // BODY) as turn:
                steps(turn)
            for c in range(TC):
                turn_out(S // BODY - 1, 1, c)

    return nc


def kernel(x, cond_2048, L0_cond_Wq, L0_cond_Wo, L1_cond_W_ih, L1_cond_W_hh, L1_cond_b_ih, L1_cond_b_hh):
    import numpy as np
    import concourse.bacc as bacc
    from concourse.bass_utils import run_bass_kernel_spmd

    x, cond = np.asarray(x), np.asarray(cond_2048)
    B, D, T = x.shape
    arrays = {
        "x": x,
        "x_t": x.transpose(2, 1, 0).reshape(T // 128, 128, D * B).transpose(1, 0, 2),
        "cond": cond,
        "h0_t": cond.T.reshape(T // 128, 128, B).transpose(1, 0, 2).reshape(128, -1),
        "wq_t": np.asarray(L0_cond_Wq).T,
        "wo_t": np.asarray(L0_cond_Wo).T,
        "w_ih": np.asarray(L1_cond_W_ih),
        "w_hh": np.asarray(L1_cond_W_hh),
        "b_ih": np.asarray(L1_cond_b_ih).reshape(-1, 128),
        "b_hh": np.asarray(L1_cond_b_hh).reshape(-1, 128),
    }
    arrays = {n: np.ascontiguousarray(a) for n, a in arrays.items()}
    nc = bacc.Bacc("TRN2", target_bir_lowering=False, num_devices=1)
    args = [nc.dram_tensor(n, a.shape, mybir.dt.from_np(a.dtype), kind="ExternalInput").ap()
            for n, a in arrays.items()]
    out = nc.dram_tensor("out", (B, D, T), mybir.dt.float32, kind="ExternalOutput").ap()
    attention_then_gru(nc, *args, out)
    result = run_bass_kernel_spmd(nc, [arrays], core_ids=[0])
    return result.results[0]["out"]
```
